# Optimizing a Trainium2 kernel written in Bass

```python
import numpy as np
import jax
import jax.numpy as jnp

def _softmax(x, axis=-1):
    return jax.nn.softmax(x, axis=axis)

def _gelu(x):
    return jax.nn.gelu(x, approximate=True)

def _silu(x):
    return jax.nn.silu(x)

def _sigmoid(x):
    return jax.nn.sigmoid(x)

def _layernorm(x, axis=-1, eps=1e-05):
    m = jnp.mean(x, axis=axis, keepdims=True)
    v = jnp.var(x, axis=axis, keepdims=True)
    return (x - m) / jnp.sqrt(v + eps)

def _scatter_add(tgt, idx, src, axis=0):
    return tgt.at[idx].add(src)

def _segment_sum(src, seg, n):
    return jax.ops.segment_sum(src, seg, n)
kernel_name = 'mk_dlrm_tower_d1_rec_r8_5d1e10'

def setup_inputs(seed: int=0):
    np.random.seed(seed)
    _w = jnp.asarray

    def _rec_inputs():
        import jax
        import jax.numpy as jnp
        _tk = jax.random.key(seed)
        ids = jnp.stack([jax.random.randint(jax.random.fold_in(_tk, 200 + f), (2048,), 0, v, jnp.int32) for f, v in enumerate([12500, 1250, 12500, 1250, 125000, 12500, 1000, 1000, 1000, 1000, 1000, 12500, 1000, 12500, 12500, 12500, 1000, 1250, 1250, 1250, 12500, 1000, 1000, 1250, 1250, 1000])], axis=1)
        tbl_0 = 0.05 * jax.random.normal(jax.random.fold_in(_tk, 500 + 0), (12500, 128), jnp.float32)
        tbl_1 = 0.05 * jax.random.normal(jax.random.fold_in(_tk, 500 + 1), (1250, 128), jnp.float32)
        tbl_2 = 0.05 * jax.random.normal(jax.random.fold_in(_tk, 500 + 2), (12500, 128), jnp.float32)
        tbl_3 = 0.05 * jax.random.normal(jax.random.fold_in(_tk, 500 + 3), (1250, 128), jnp.float32)
        tbl_4 = 0.05 * jax.random.normal(jax.random.fold_in(_tk, 500 + 4), (125000, 128), jnp.float32)
        tbl_5 = 0.05 * jax.random.normal(jax.random.fold_in(_tk, 500 + 5), (12500, 128), jnp.float32)
        tbl_6 = 0.05 * jax.random.normal(jax.random.fold_in(_tk, 500 + 6), (1000, 128), jnp.float32)
        tbl_7 = 0.05 * jax.random.normal(jax.random.fold_in(_tk, 500 + 7), (1000, 128), jnp.float32)
        tbl_8 = 0.05 * jax.random.normal(jax.random.fold_in(_tk, 500 + 8), (1000, 128), jnp.float32)
        tbl_9 = 0.05 * jax.random.normal(jax.random.fold_in(_tk, 500 + 9), (1000, 128), jnp.float32)
        tbl_10 = 0.05 * jax.random.normal(jax.random.fold_in(_tk, 500 + 10), (1000, 128), jnp.float32)
        tbl_11 = 0.05 * jax.random.normal(jax.random.fold_in(_tk, 500 + 11), (12500, 128), jnp.float32)
        tbl_12 = 0.05 * jax.random.normal(jax.random.fold_in(_tk, 500 + 12), (1000, 128), jnp.float32)
        tbl_13 = 0.05 * jax.random.normal(jax.random.fold_in(_tk, 500 + 13), (12500, 128), jnp.float32)
        tbl_14 = 0.05 * jax.random.normal(jax.random.fold_in(_tk, 500 + 14), (12500, 128), jnp.float32)
        tbl_15 = 0.05 * jax.random.normal(jax.random.fold_in(_tk, 500 + 15), (12500, 128), jnp.float32)
        tbl_16 = 0.05 * jax.random.normal(jax.random.fold_in(_tk, 500 + 16), (1000, 128), jnp.float32)
        tbl_17 = 0.05 * jax.random.normal(jax.random.fold_in(_tk, 500 + 17), (1250, 128), jnp.float32)
        tbl_18 = 0.05 * jax.random.normal(jax.random.fold_in(_tk, 500 + 18), (1250, 128), jnp.float32)
        tbl_19 = 0.05 * jax.random.normal(jax.random.fold_in(_tk, 500 + 19), (1250, 128), jnp.float32)
        tbl_20 = 0.05 * jax.random.normal(jax.random.fold_in(_tk, 500 + 20), (12500, 128), jnp.float32)
        tbl_21 = 0.05 * jax.random.normal(jax.random.fold_in(_tk, 500 + 21), (1000, 128), jnp.float32)
        tbl_22 = 0.05 * jax.random.normal(jax.random.fold_in(_tk, 500 + 22), (1000, 128), jnp.float32)
        tbl_23 = 0.05 * jax.random.normal(jax.random.fold_in(_tk, 500 + 23), (1250, 128), jnp.float32)
        tbl_24 = 0.05 * jax.random.normal(jax.random.fold_in(_tk, 500 + 24), (1250, 128), jnp.float32)
        tbl_25 = 0.05 * jax.random.normal(jax.random.fold_in(_tk, 500 + 25), (1000, 128), jnp.float32)
        _rk = jax.random.fold_in(_tk, 7)
        r_bottom_output = -0.000520686 + 1.00062 * jax.random.normal(jax.random.fold_in(_rk, 101), (2048, 128), jnp.float32)
        W_top1 = 0.0456912 * jax.random.normal(jax.random.fold_in(_tk, 801), (479, 512), jnp.float32)
        W_top2 = 0.0441942 * jax.random.normal(jax.random.fold_in(_tk, 802), (512, 256), jnp.float32)
        W_top3 = 0.0625 * jax.random.normal(jax.random.fold_in(_tk, 803), (256, 1), jnp.float32)
        b_top1 = jnp.zeros((512,), jnp.float32)
        b_top2 = jnp.zeros((256,), jnp.float32)
        return (r_bottom_output, ids, tbl_0, tbl_1, tbl_2, tbl_3, tbl_4, tbl_5, tbl_6, tbl_7, tbl_8, tbl_9, tbl_10, tbl_11, tbl_12, tbl_13, tbl_14, tbl_15, tbl_16, tbl_17, tbl_18, tbl_19, tbl_20, tbl_21, tbl_22, tbl_23, tbl_24, tbl_25, W_top1, b_top1, W_top2, b_top2, W_top3)
    r_bottom_output, ids, tbl_0, tbl_1, tbl_2, tbl_3, tbl_4, tbl_5, tbl_6, tbl_7, tbl_8, tbl_9, tbl_10, tbl_11, tbl_12, tbl_13, tbl_14, tbl_15, tbl_16, tbl_17, tbl_18, tbl_19, tbl_20, tbl_21, tbl_22, tbl_23, tbl_24, tbl_25, W_top1, b_top1, W_top2, b_top2, W_top3 = _rec_inputs()

    def _L0_rec_setup():
        import jax, jax.numpy as jnp
        import numpy as np
        NUM_FEATURES = 27
        _TRIU_I, _TRIU_J = np.triu_indices(NUM_FEATURES, k=1)
        key = jax.random.key(seed)
        k1, k2 = jax.random.split(key)
        bottom_output = jax.random.normal(k1, (2048, 128), dtype=jnp.float32)
        embeddings = jax.random.normal(k2, (2048, 26, 128), dtype=jnp.float32)
        return {'bottom_output': bottom_output, 'embeddings': embeddings}
    _L0_rec_all = _L0_rec_setup()
    _L0_rec_in = {k: v for k, v in _L0_rec_all.items() if k in ()}
    del _L0_rec_all
    return {'r_bottom_output': r_bottom_output, 'ids': ids, 'tbl_0': tbl_0, 'tbl_1': tbl_1, 'tbl_2': tbl_2, 'tbl_3': tbl_3, 'tbl_4': tbl_4, 'tbl_5': tbl_5, 'tbl_6': tbl_6, 'tbl_7': tbl_7, 'tbl_8': tbl_8, 'tbl_9': tbl_9, 'tbl_10': tbl_10, 'tbl_11': tbl_11, 'tbl_12': tbl_12, 'tbl_13': tbl_13, 'tbl_14': tbl_14, 'tbl_15': tbl_15, 'tbl_16': tbl_16, 'tbl_17': tbl_17, 'tbl_18': tbl_18, 'tbl_19': tbl_19, 'tbl_20': tbl_20, 'tbl_21': tbl_21, 'tbl_22': tbl_22, 'tbl_23': tbl_23, 'tbl_24': tbl_24, 'tbl_25': tbl_25, 'W_top1': W_top1, 'b_top1': b_top1, 'W_top2': W_top2, 'b_top2': b_top2, 'W_top3': W_top3}

def reference(r_bottom_output, ids, tbl_0, tbl_1, tbl_2, tbl_3, tbl_4, tbl_5, tbl_6, tbl_7, tbl_8, tbl_9, tbl_10, tbl_11, tbl_12, tbl_13, tbl_14, tbl_15, tbl_16, tbl_17, tbl_18, tbl_19, tbl_20, tbl_21, tbl_22, tbl_23, tbl_24, tbl_25, W_top1, b_top1, W_top2, b_top2, W_top3):
    import jax
    import jax.numpy as jnp

    def _L0_rec_ref(bottom_output, embeddings):
        import jax, jax.numpy as jnp
        import numpy as np
        NUM_FEATURES = 27
        _TRIU_I, _TRIU_J = np.triu_indices(NUM_FEATURES, k=1)
        all_emb = jnp.concatenate([bottom_output[:, None, :], embeddings], axis=1)
        gram = jnp.einsum('bfd,bgd->bfg', all_emb, all_emb)
        return gram[:, _TRIU_I, _TRIU_J]
    e = jnp.stack([tbl_0[ids[:, 0]], tbl_1[ids[:, 1]], tbl_2[ids[:, 2]], tbl_3[ids[:, 3]], tbl_4[ids[:, 4]], tbl_5[ids[:, 5]], tbl_6[ids[:, 6]], tbl_7[ids[:, 7]], tbl_8[ids[:, 8]], tbl_9[ids[:, 9]], tbl_10[ids[:, 10]], tbl_11[ids[:, 11]], tbl_12[ids[:, 12]], tbl_13[ids[:, 13]], tbl_14[ids[:, 14]], tbl_15[ids[:, 15]], tbl_16[ids[:, 16]], tbl_17[ids[:, 17]], tbl_18[ids[:, 18]], tbl_19[ids[:, 19]], tbl_20[ids[:, 20]], tbl_21[ids[:, 21]], tbl_22[ids[:, 22]], tbl_23[ids[:, 23]], tbl_24[ids[:, 24]], tbl_25[ids[:, 25]]], axis=1)
    z = _L0_rec_ref(r_bottom_output, e)
    z = z.reshape(z.shape[0], -1)
    h = jnp.concatenate([z, r_bottom_output], axis=1)
    h = jnp.maximum(h @ W_top1 + b_top1, 0.0)
    h = jnp.maximum(h @ W_top2 + b_top2, 0.0)
    y = h @ W_top3
    return y

_drawn_inputs = setup_inputs


def setup_inputs(seed=0):
    import zlib

    import numpy as np

    out = dict(_drawn_inputs(seed))
    spreads = {'b_top1': (0.0, 0.1), 'b_top2': (0.0, 0.1)}
    factors = {}
    for name, (base, spread) in spreads.items():
        noise = np.random.default_rng([zlib.crc32(name.encode()), seed]).standard_normal(out[name].shape)
        drawn = base * np.exp(spread * noise) if base else spread * noise
        out[name] = jnp.asarray(drawn.astype(out[name].dtype))
    for name, factor in factors.items():
        out[name] = (out[name] * factor).astype(out[name].dtype)
    return out
```

```python
import concourse.bass as bass
from concourse import mybir
from contextlib import ExitStack

TABLES = 26
F = TABLES + 1
D = 128
BATCH = 2048
N1, N2 = 512, 256

S, J = 4, 64
BLOCK = S * J
BLOCKS = BATCH // BLOCK
HALVES = BLOCK // 128
FW = 32
GW = F - 1

ONEHOT = [(6, 7), (8, 9), (10, 12)]
VP, VK = 125, 8
ROWS = [(0, 1), (2, 3), (4, 5), (11, 13), (14, 15), (16, 17), (18, 19), (20, 21), (22, 23), (24, 25)]
NO, NR = len(ONEHOT), len(ROWS)

GROUPS = [(g, 3) for g in range(1, 25, 3)] + [(25, 2)]


def group_columns():
    at, out = 0, []
    for g, n in GROUPS:
        out.append(at)
        at += n * (g + n - 1)
    return out, at


GROUP_AT, ZUSED = group_columns()
ZC = 3
ZW = ZC * 128

A_UNITS = [("onehot", 0), ("rows", 0), ("rows", 1), ("onehot", 1), ("bottom", 0), ("rows", 2), ("rows", 3),
           ("onehot", 2), ("rows", 4), ("rows", 5), ("rows", 6), ("rows", 7), ("rows", 8), ("rows", 9)]
C_UNITS = [("columns", q) for q in range(9)] + [("chunk", c) for c in range(ZC)] + \
          [("layer1", 0), ("layer1", 1), ("layer2", 0), ("layer3", 0)]
NA, NC = len(A_UNITS) // 2, len(C_UNITS) // 2
GSETS = 8
NG = GSETS // 2

STEPS = [("A", 0)] + [("C", 0), ("C", 1), ("C", 2), ("A", 1), ("C", 3), ("C", 4), ("C", 5), ("A", 2),
         ("C", 6), ("C", 7), ("C", 8), ("C", 9), ("C", 10), ("C", 11), ("A", 3), ("C", 12), ("C", 13),
         ("A", 4), ("A", 5), ("A", 6), ("C", 14), ("A", 7), ("C", 15)] + [("A", u) for u in range(8, 14)] + \
        [("B", k) for k in range(GSETS)]


def dlrm_tower(nc, bottom, ids, ids_by_table, tables, w1, b1, w2, b2, w3, identity, vocab, out):
    fp32, bf16, i32 = mybir.dt.float32, mybir.dt.bfloat16, mybir.dt.int32
    ALU = mybir.AluOpType
    ACT = mybir.ActivationFunctionType

    ctx = ExitStack()
    with ctx:
        def sb(name, shape, dt=fp32):
            return ctx.enter_context(nc.sbuf_tensor(name, shape, dt))

        def pb(name, shape):
            return ctx.enter_context(nc.psum_tensor(name, shape, fp32))

        def sem(name):
            return ctx.enter_context(nc.semaphore(name))

        idx = [sb(f"idx{i}", [128, HALVES, TABLES], i32) for i in range(2)]
        rows = sb("rows", [128, NR, 2, HALVES, D])
        bottom_rows = sb("bottom_rows", [128, HALVES, D])
        ids_bc = sb("ids_bc", [128, NO, 2, BLOCK], i32)
        onehot = sb("onehot", [128, NO, 2, VK, BLOCK], bf16)
        table_raw = sb("table_raw", [128, 2 * NO, VK * D])
        table_hi = sb("table_hi", [128, 2 * NO, VK * D], bf16)
        table_mid = sb("table_mid", [128, 2 * NO, VK * D], bf16)
        table_lo = sb("table_lo", [128, 2 * NO, VK * D], bf16)
        vocab_sb = sb("vocab_sb", [128, VK])
        ident = sb("ident", [128, 128])
        XT = sb("XT", [128, J, S, FW])
        bottom_T = sb("bottom_T", [128, BLOCK])
        gram = sb("gram", [128, J, GW])
        pairs = sb("pairs", [J, S, ZW])
        pairs_T = sb("pairs_T", [128, ZC, BLOCK])
        h1 = sb("h1", [128, N1 // 128, BLOCK])
        h2 = sb("h2", [128, N2 // 128, BLOCK])
        y = sb("y", [1, BATCH])
        w1_sb = sb("w1_sb", [128, N1 // 128, N1])
        w2_sb = sb("w2_sb", [128, N1 // 128, N2])
        w3_sb = sb("w3_sb", [128, N2 // 128])
        b1_sb = sb("b1_sb", [128, N1 // 128])
        b2_sb = sb("b2_sb", [128, N2 // 128])

        psA = [pb(f"psA{i}", [128, 512]) for i in range(2)]
        psG = [pb(f"psG{i}", [128, 2, 512]) for i in range(2)]
        psC = [pb(f"psC{i}", [128, 512]) for i in range(2)]

        idx_ready = [sem(f"idx_ready{i}") for i in range(2)]
        rows_ready = [sem(f"rows_ready{p}") for p in range(NR)]
        bottom_ready = sem("bottom_ready")
        ids_ready = [sem(f"ids_ready{i}") for i in range(NO)]
        onehot_made = sem("onehot_made")
        table_ready = [sem(f"table_ready{i}") for i in range(2 * NO)]
        hi_made = sem("hi_made")
        rest_made = sem("rest_made")
        mid_made = sem("mid_made")
        table_split = sem("table_split")
        consts_ready = sem("consts_ready")
        vocab_ready = sem("vocab_ready")
        weights_ready = sem("weights_ready")
        pads_set = sem("pads_set")
        a_full = [sem(f"a_full{i}") for i in range(2)]
        a_done = [sem(f"a_done{i}") for i in range(2)]
        g_full = [sem(f"g_full{i}") for i in range(2)]
        g_done = [sem(f"g_done{i}") for i in range(2)]
        c_full = [sem(f"c_full{i}") for i in range(2)]
        c_done = [sem(f"c_done{i}") for i in range(2)]
        out_done = sem("out_done")

        XT_by_feature = XT[:, :, :, :].rearrange("p j s f -> p f s j")

        def features(kind, n):
            if kind == "bottom":
                return 0, 0, 1
            a, b = (ONEHOT if kind == "onehot" else ROWS)[n]
            return a + 1, b + 1, b - a

        def unit_count(kind, n, m):
            u = A_UNITS.index((kind, n))
            return u % 2, m * NA + (u // 2 + 1)

        def a_signal(kind, n, m):
            bank, count = unit_count(kind, n, m)
            return a_full[bank], count

        def as_register(engine, count):
            return count if isinstance(count, int) else engine.to_reg(count)

        block = ctx.enter_context(nc.Block())

        @block.sync
        def _(sp):
            def load_idx(m, at, parity):
                sp.dma_start(idx[parity][:, :, :], ids[bass.ds(at, BLOCK), :].rearrange(
                    "(h p) f -> p h f", p=128)).then_inc(idx_ready[parity], 16)

            def load_bottom(at):
                sp.dma_start(bottom_rows[:, :, :], bottom[bass.ds(at, BLOCK), :].rearrange(
                    "(h p) d -> p h d", p=128)).then_inc(bottom_ready, 16)

            def load_ids(i, at):
                a, b = ONEHOT[i]
                sp.dma_start(ids_bc[:, i, :, :], ids_by_table[a:b + 1:b - a, bass.ds(at, BLOCK)]
                             .partition_broadcast(128)).then_inc(ids_ready[i], 16)

            for m in range(2):
                load_idx(m, m * BLOCK, m)
            sp.dma_start(vocab_sb[0:VP, :], vocab).then_inc(vocab_ready, 16)
            for n, t in enumerate(t for pair in ONEHOT for t in pair):
                src = tables[t].rearrange("(p k) d -> p (k d)", k=VK)
                sp.dma_start(table_raw[0:112, n, :], src[0:112, :]).then_inc(table_ready[n], 16)
                sp.dma_start(table_raw[112:VP, n, :], src[112:VP, :]).then_inc(table_ready[n], 16)
                if n < NO:
                    load_ids(n, 0)
            sp.dma_start(ident[:, :], identity).then_inc(consts_ready, 16)
            load_bottom(0)
            sp.dma_start(w1_sb[:, :, :], w1.rearrange("(t p) n -> p t n", p=128)).then_inc(weights_ready, 16)
            sp.dma_start(w2_sb[:, :, :], w2.rearrange("(t p) n -> p t n", p=128)).then_inc(weights_ready, 16)
            sp.dma_start(w3_sb[:, :], w3).then_inc(weights_ready, 16)
            sp.dma_start(b1_sb[:, :], b1).then_inc(weights_ready, 16)
            sp.dma_start(b2_sb[:, :], b2).then_inc(weights_ready, 16)
            for i in range(2):
                sp.wait_ge(onehot_made, i + 1)
                load_ids(i, BLOCK)

            def refill(m, parity, more=2):
                if more >= 1:
                    sp.wait_ge(onehot_made, m * NO + 3)
                    load_ids(2, (m + 1) * BLOCK)
                    sp.wait_ge(*a_signal("bottom", 0, m))
                    load_bottom((m + 1) * BLOCK)
                if more >= 2:
                    for i in range(2):
                        sp.wait_ge(onehot_made, m * NO + 4 + i)
                        load_ids(i, (m + 2) * BLOCK)
                    sp.wait_ge(rows_ready[NR - 1], (m + 1) * 64)
                    load_idx(m + 2, (m + 2) * BLOCK, parity)

            with sp.Fori(0, BLOCKS // 2 - 1) as i:
                refill(i * 2, 0)
                refill(i * 2 + 1, 1)
            refill(BLOCKS - 2, 0, 1)
            sp.wait_ge(c_done[1], BLOCKS * NC)
            sp.dma_start(out.rearrange("b o -> o b"), y[0:1, :]).then_inc(out_done, 16)
            sp.wait_ge(out_done, 16)

        @block.gpsimd
        def _(pool):
            def gather_block(m, parity, visit, reuse=True):
                pool.wait_ge(idx_ready[parity], (visit + 1) * 16)
                for p, pair in enumerate(ROWS):
                    if reuse:
                        bank, count = unit_count("rows", p, m - 1)
                        count = as_register(pool, count)
                        pool.wait_ge(idx_ready[parity], 16)
                        pool.wait_ge(a_full[bank], count)
                    for n, t in enumerate(pair):
                        for h in range(HALVES):
                            nc.gpsimd.indirect_dma_start(
                                rows[:, p, n, h, :], None, tables[t],
                                bass.IndirectOffsetOnAxis(ap=idx[parity][:, h, t:t + 1], axis=0),
                            ).then_inc(rows_ready[p], 16)

            gather_block(0, 0, 0, reuse=False)
            gather_block(1, 1, 0)
            with pool.Fori(1, BLOCKS // 2) as i:
                gather_block(i * 2, 0, i)
                gather_block(i * 2 + 1, 1, i)

        @block.tensor
        def _(pe):
            def phase_a(u, m, first):
                kind, n = A_UNITS[u]
                bank = psA[u % 2]
                if not first or u >= 2:
                    pe.wait_ge(a_done[u % 2], m * NA + u // 2)
                if kind == "onehot":
                    if first:
                        pe.wait_ge(table_split, 2 * n + 2)
                    pe.wait_ge(onehot_made, m * NO + n + 1)
                    for i in range(2):
                        parts = [x for k in range(VK) for x in ((table_hi, k), (table_mid, k), (table_lo, k))]
                        for q, (part, k) in enumerate(parts):
                            last = nc.tensor.matmul(bank[:, i * BLOCK:(i + 1) * BLOCK],
                                                    part[0:VP, 2 * n + i, k * D:(k + 1) * D],
                                                    onehot[0:VP, n, i, k, :],
                                                    start=(q == 0), stop=(q == len(parts) - 1))
                    last.then_inc(a_full[u % 2], 1)
                elif kind == "bottom":
                    if first:
                        pe.wait_ge(consts_ready, 16)
                    pe.wait_ge(bottom_ready, (m + 1) * 16)
                    for h in range(HALVES):
                        last = nc.tensor.transpose(bank[:, h * 128:(h + 1) * 128], bottom_rows[:, h, :], ident[:, :])
                    last.then_inc(a_full[u % 2], 1)
                else:
                    if first:
                        pe.wait_ge(consts_ready, 16)
                    pe.wait_ge(rows_ready[n], (m + 1) * 64)
                    for i in range(2):
                        for h in range(HALVES):
                            last = nc.tensor.transpose(bank[:, (i * HALVES + h) * 128:(i * HALVES + h + 1) * 128],
                                                       rows[:, n, i, h, :], ident[:, :])
                    last.then_inc(a_full[u % 2], 1)

            def phase_b(k, m, first):
                if k == 0:
                    for i in range(2):
                        pe.wait_ge(a_done[i], (m + 1) * NA)
                    if first:
                        pe.wait_ge(pads_set, 1)
                if not first or k >= 2:
                    pe.wait_ge(g_done[k % 2], m * NG + k // 2)
                for i in range(8):
                    last = nc.tensor.matmul(psG[k % 2][:, i // 4, (i % 4) * S * GW:(i % 4 + 1) * S * GW],
                                            XT[:, 8 * k + i, :, :].rearrange("p s f -> p (s f)"), XT[:, 8 * k + i, :, 1:F],
                                            start=True, stop=True)
                last.then_inc(g_full[k % 2], 1)

            def phase_c(u, m, first):
                kind, n = C_UNITS[u]
                bank = psC[u % 2]
                bank_free = as_register(pe, m * NC + u // 2)
                if kind == "columns":
                    grams_there = as_register(pe, (m + 1) * NG)
                    pe.wait_ge(consts_ready, 16)
                    if n == 0:
                        for i in range(2):
                            pe.wait_ge(g_done[i], grams_there)
                elif kind == "chunk":
                    columns_there = [as_register(pe, m * NC + 5 - i) for i in range(2)]
                    pe.wait_ge(pads_set, 1)
                    if n == 0:
                        for i in range(2):
                            pe.wait_ge(c_done[i], columns_there[i])
                if not first or u >= 2:
                    pe.wait_ge(c_done[u % 2], bank_free)
                if kind == "columns":
                    g0, count = GROUPS[n]
                    for i in range(count):
                        last = nc.tensor.transpose(bank[0:J, i * 128:(i + 1) * 128], gram[:, :, g0 - 1 + i], ident[:, :])
                elif kind == "chunk":
                    for s in range(S):
                        last = nc.tensor.transpose(bank[:, s * J:(s + 1) * J], pairs[:, s, n * 128:(n + 1) * 128],
                                                   ident[0:J, 0:J])
                elif kind == "layer1":
                    if n == 0:
                        if first:
                            pe.wait_ge(weights_ready, 5 * 16)
                        pe.wait_ge(c_done[0], m * NC + 6)
                        pe.wait_ge(c_done[1], m * NC + 6)
                    for i in range(2):
                        for t in range(ZC + 1):
                            last = nc.tensor.matmul(bank[:, i * BLOCK:(i + 1) * BLOCK],
                                                    w1_sb[:, t, (2 * n + i) * 128:(2 * n + i + 1) * 128],
                                                    pairs_T[:, t, :] if t < ZC else bottom_T[:, :],
                                                    start=(t == 0), stop=(t == ZC))
                elif kind == "layer2":
                    pe.wait_ge(c_done[0], m * NC + 7)
                    pe.wait_ge(c_done[1], m * NC + 7)
                    for i in range(2):
                        for t in range(N1 // 128):
                            last = nc.tensor.matmul(bank[:, i * BLOCK:(i + 1) * BLOCK],
                                                    w2_sb[:, t, i * 128:(i + 1) * 128], h1[:, t, :],
                                                    start=(t == 0), stop=(t == N1 // 128 - 1))
                else:
                    pe.wait_ge(c_done[0], m * NC + 8)
                    for t in range(N2 // 128):
                        last = nc.tensor.matmul(bank[0:1, 0:BLOCK], w3_sb[:, t:t + 1], h2[:, t, :],
                                                start=(t == 0), stop=(t == N2 // 128 - 1))
                last.then_inc(c_full[u % 2], 1)

            def block_steps(m, first=False, second=False):
                for phase, u in STEPS:
                    if phase == "A":
                        phase_a(u, m, first)
                    elif phase == "B":
                        phase_b(u, m, first)
                    elif not first:
                        phase_c(u, m - 1, second)

            block_steps(0, first=True)
            block_steps(1, second=True)
            with pe.Fori(2, BLOCKS) as m:
                block_steps(m)
            for u in range(len(C_UNITS)):
                phase_c(u, BLOCKS - 1, False)

        def gram_views(k, s):
            lanes = slice(FW * s, FW * (s + 1))
            src = psG[k % 2][lanes, :, 0:4 * S * GW].rearrange("p b (j s g) -> p b j s g", s=S, g=GW)[:, :, :, s, :]
            dst = gram[lanes, 8 * k:8 * k + 8, :].rearrange("p (b j) g -> p b j g", b=2)
            return dst, src

        def pair_views(n):
            g0, count = GROUPS[n]
            width = g0 + count - 1
            src = psC[n % 2][0:J, 0:count * 128].rearrange("p (g s f) -> p g s f", s=S, f=FW)[:, :, :, 0:width]
            dst = pairs[:, :, GROUP_AT[n]:GROUP_AT[n] + count * width].rearrange("p s (g f) -> p g s f", g=count)
            return dst, src

        def xt_views(u):
            a, b, step = features(*A_UNITS[u])
            count = 1 if a == b else 2
            src = psA[u % 2][:, 0:count * BLOCK].rearrange("p (f s j) -> p f s j", s=S, j=J)
            return XT_by_feature[:, a:b + 1:step, :, :], src

        @block.vector
        def _(dve):
            nc.vector.memset(XT[:, :, :, F:], 0.0)
            nc.vector.memset(pairs[:, :, ZUSED:], 0.0).then_inc(pads_set, 1)

            def make_onehot(i, m, first=False):
                dve.wait_ge(ids_ready[i], (m + 1) * 16)
                if not first:
                    dve.wait_ge(*a_signal("onehot", i, m - 1))
                for n in range(2):
                    for k in range(VK):
                        last = nc.vector.tensor_scalar(onehot[0:VP, i, n, k, :], ids_bc[0:VP, i, n, :],
                                                       vocab_sb[0:VP, k:k + 1], None, ALU.is_equal)
                last.then_inc(onehot_made, 1)

            def split_table(n):
                dve.wait_ge(hi_made, n + 1)
                nc.vector.tensor_tensor(table_raw[0:VP, n, :], table_raw[0:VP, n, :], table_hi[0:VP, n, :],
                                        ALU.subtract).then_inc(rest_made, 1)
                dve.wait_ge(mid_made, n + 1)
                nc.vector.tensor_tensor(table_lo[0:VP, n, :], table_raw[0:VP, n, :], table_mid[0:VP, n, :],
                                        ALU.subtract).then_inc(table_split, 1)

            for n in range(2):
                split_table(n)
            dve.wait_ge(vocab_ready, 16)
            make_onehot(0, 0, first=True)
            for n in range(2, 2 * NO):
                split_table(n)
            make_onehot(1, 0, first=True)

            def phase_a(u, m):
                dve.wait_ge(a_full[0], m * NA + u // 2 + 1)
                dst, src = xt_views(u)
                if A_UNITS[u][0] == "bottom":
                    nc.vector.tensor_copy(bottom_T[:, :], psA[0][:, 0:BLOCK])
                nc.vector.tensor_copy(dst, src).then_inc(a_done[0], 1)

            def phase_b(k, m):
                dve.wait_ge(g_full[0], m * NG + k // 2 + 1)
                for s in range(S):
                    dst, src = gram_views(k, s)
                    last = nc.vector.tensor_copy(dst, src)
                last.then_inc(g_done[0], 1)

            def phase_c(u, m):
                kind, n = C_UNITS[u]
                dve.wait_ge(c_full[0], m * NC + u // 2 + 1)
                if kind == "columns":
                    dst, src = pair_views(n)
                    last = nc.vector.tensor_copy(dst, src)
                elif kind == "chunk":
                    last = nc.vector.tensor_copy(pairs_T[:, n, :], psC[0][:, 0:BLOCK])
                else:
                    h, bias = (h1, b1_sb) if kind == "layer1" else (h2, b2_sb)
                    for i in range(2):
                        last = nc.vector.tensor_scalar(h[:, 2 * n + i, :], psC[0][:, i * BLOCK:(i + 1) * BLOCK],
                                                       bias[:, 2 * n + i:2 * n + i + 1], 0.0, ALU.add, ALU.max)
                last.then_inc(c_done[0], 1)

            def block_steps(m, first=False, second=False, final=False):
                if second:
                    dve.wait_ge(weights_ready, 5 * 16)
                for phase, u in STEPS:
                    if phase == "A":
                        kind, n = A_UNITS[u]
                        if kind == "onehot":
                            if n == 0:
                                make_onehot(2, m, first)
                            elif not final:
                                make_onehot(n - 1, m + 1)
                        if u % 2 == 0:
                            phase_a(u, m)
                    elif phase == "B":
                        if u % 2 == 0:
                            phase_b(u, m)
                    elif not first and u % 2 == 0:
                        phase_c(u, m - 1)

            block_steps(0, first=True)
            block_steps(1, second=True)
            with dve.Fori(2, BLOCKS - 1) as m:
                block_steps(m)
            block_steps(BLOCKS - 1, final=True)
            for u in range(0, len(C_UNITS), 2):
                phase_c(u, BLOCKS - 1)

        @block.scalar
        def _(act):
            for n in range(2 * NO):
                act.wait_ge(table_ready[n], 32)
                nc.scalar.copy(table_hi[0:VP, n, :], table_raw[0:VP, n, :]).then_inc(hi_made, 1)
                act.wait_ge(rest_made, n + 1)
                nc.scalar.copy(table_mid[0:VP, n, :], table_raw[0:VP, n, :]).then_inc(mid_made, 1)

            def phase_a(u, m):
                act.wait_ge(a_full[1], m * NA + u // 2 + 1)
                dst, src = xt_views(u)
                nc.scalar.copy(dst, src).then_inc(a_done[1], 1)

            def phase_b(k, m):
                act.wait_ge(g_full[1], m * NG + k // 2 + 1)
                for s in range(S):
                    dst, src = gram_views(k, s)
                    last = nc.scalar.copy(dst, src)
                last.then_inc(g_done[1], 1)

            def phase_c(u, m):
                kind, n = C_UNITS[u]
                act.wait_ge(c_full[1], m * NC + u // 2 + 1)
                if kind == "columns":
                    dst, src = pair_views(n)
                    last = nc.scalar.copy(dst, src)
                elif kind == "chunk":
                    last = nc.scalar.copy(pairs_T[:, n, :], psC[1][:, 0:BLOCK])
                elif kind == "layer1":
                    for i in range(2):
                        last = nc.scalar.activation(h1[:, 2 * n + i, :], psC[1][:, i * BLOCK:(i + 1) * BLOCK],
                                                    ACT.Relu, bias=b1_sb[:, 2 * n + i:2 * n + i + 1])
                else:
                    last = nc.scalar.copy(y[0:1, bass.ds(m * BLOCK, BLOCK)], psC[1][0:1, 0:BLOCK])
                last.then_inc(c_done[1], 1)

            def block_steps(m, first=False, second=False):
                if second:
                    act.wait_ge(weights_ready, 5 * 16)
                for phase, u in STEPS:
                    if u % 2 == 1:
                        if phase == "A":
                            phase_a(u, m)
                        elif phase == "B":
                            phase_b(u, m)
                        elif not first:
                            phase_c(u, m - 1)

            block_steps(0, first=True)
            block_steps(1, second=True)
            with act.Fori(2, BLOCKS) as m:
                block_steps(m)
            for u in range(1, len(C_UNITS), 2):
                phase_c(u, BLOCKS - 1)


def w1_rows():
    rows = [-1] * ZW
    for (g0, count), at in zip(GROUPS, GROUP_AT):
        width = g0 + count - 1
        for i in range(count):
            for f in range(g0 + i):
                rows[at + i * width + f] = f * F - f * (f + 1) // 2 + (g0 + i - f - 1)
    pairs = F * (F - 1) // 2
    return rows + list(range(pairs, pairs + D))


def kernel(**inputs):
    import numpy as np
    import concourse.bacc as bacc
    from concourse.bass_utils import run_bass_kernel_spmd as run

    nc = bacc.Bacc("TRN2", target_bir_lowering=False, num_devices=1)
    src = np.array(w1_rows())
    w1 = np.zeros((ZW + D, N1), inputs["W_top1"].dtype)
    w1[src >= 0] = np.asarray(inputs["W_top1"])[src[src >= 0]]
    arrays = {
        "bottom": inputs["r_bottom_output"],
        "ids": inputs["ids"],
        "ids_by_table": np.asarray(inputs["ids"]).T,
        **{f"tbl_{t}": inputs[f"tbl_{t}"] for t in range(TABLES)},
        "w1": w1,
        "b1": np.asarray(inputs["b_top1"]).reshape(N1 // 128, 128).T,
        "w2": inputs["W_top2"],
        "b2": np.asarray(inputs["b_top2"]).reshape(N2 // 128, 128).T,
        "w3": np.asarray(inputs["W_top3"]).reshape(N2 // 128, 128).T,
        "identity": np.eye(128, dtype=np.float32),
        "vocab": np.arange(VP * VK, dtype=np.float32).reshape(VP, VK),
    }
    arrays = {f"in_{k}": np.ascontiguousarray(a) for k, a in arrays.items()}
    aps = {k[3:]: nc.dram_tensor(k, a.shape, mybir.dt.from_np(a.dtype), kind="ExternalInput").ap()
           for k, a in arrays.items()}
    out = nc.dram_tensor("out_y", (BATCH, 1), mybir.dt.float32, kind="ExternalOutput").ap()
    dlrm_tower(nc, aps["bottom"], aps["ids"], aps["ids_by_table"], [aps[f"tbl_{t}"] for t in range(TABLES)],
               aps["w1"], aps["b1"], aps["w2"], aps["b2"], aps["w3"], aps["identity"], aps["vocab"], out)
    return run(nc, [arrays], core_ids=[0]).results[0]["out_y"]
```

```python
import concourse.bass as bass
from concourse import mybir
from contextlib import ExitStack

TABLES = 26
F = TABLES + 1
D = 128
BATCH = 2048
N1, N2 = 512, 256

S, J = 4, 64
BLOCK = S * J
BLOCKS = BATCH // BLOCK
HALVES = BLOCK // 128
FW = 32
GW = F - 1

ONEHOT = [6, 7, 8, 9, 10, 12]
VP, VK = 125, 8
RING = 3
ROWS = [(0, 1), (2, 3), (4, 5), (11, 13), (14, 15), (16, 17), (18, 19), (20, 21), (22, 23), (24, 25)]
NO, NR = len(ONEHOT), len(ROWS)

GROUPS = [(g, 3) for g in range(1, 25, 3)] + [(25, 2)]


def group_columns():
    at, out = 0, []
    for g, n in GROUPS:
        out.append(at)
        at += n * (g + n - 1)
    return out, at


GROUP_AT, ZUSED = group_columns()
ZC = 3
ZW = ZC * 128

A_UNITS = [[("onehot", 0), ("onehot", 1), ("bottom", 0), ("onehot", 2)], [("rows", p) for p in range(NR)]]
NA = [len(units) for units in A_UNITS]
C_UNITS = [("columns", q) for q in range(9)] + [("chunk", c) for c in range(ZC)] + \
          [("layer1", 0), ("layer1", 1), ("layer2", 0), ("layer3", 0)]
NC = len(C_UNITS) // 2
GSETS = 8

STEPS = [("onehot", 0), ("C", 0), ("C", 1), ("rows", 0), ("C", 2), ("C", 3), ("onehot", 1), ("C", 4), ("C", 5),
         ("rows", 1), ("C", 6), ("C", 7), ("onehot", 2), ("C", 8), ("rows", 2), ("C", 9),
         ("C", 10), ("C", 11), ("rows", 3), ("C", 12), ("rows", 4), ("C", 13), ("onehot", 3), ("rows", 5),
         ("bottom", 0), ("C", 14), ("rows", 6), ("rows", 7), ("onehot", 4), ("rows", 8), ("onehot", 5), ("rows", 9),
         ("C", 15)] + [("B", k) for k in range(GSETS)]
MAKE = {("C", 12): [(3, 0), (4, 0)], ("C", 14): [(5, 0), (0, 1)], ("B", 0): [(1, 1)], ("B", 4): [(2, 1)]}
NOT_MADE_AHEAD = 3


def dlrm_tower(nc, bottom, ids, ids_by_table, tables, w1, b1, w2, b2, w3, identity, vocab, out):
    fp32, fp32r, i32 = mybir.dt.float32, mybir.dt.float32r, mybir.dt.int32
    ALU = mybir.AluOpType
    ACT = mybir.ActivationFunctionType

    ctx = ExitStack()
    with ctx:
        def sb(name, shape, dt=fp32):
            return ctx.enter_context(nc.sbuf_tensor(name, shape, dt))

        def pb(name, shape):
            return ctx.enter_context(nc.psum_tensor(name, shape, fp32))

        def sem(name):
            return ctx.enter_context(nc.semaphore(name))

        idx = [sb(f"idx{i}", [128, HALVES, TABLES], i32) for i in range(2)]
        rows = sb("rows", [128, NR, 2, HALVES, D])
        bottom_rows = sb("bottom_rows", [128, HALVES, D])
        ids_bc = sb("ids_bc", [128, NO, BLOCK], i32)
        onehot = sb("onehot", [128, RING, VK, BLOCK], fp32r)
        table_raw = sb("table_raw", [128, 2, VK * D])
        table_hi = sb("table_hi", [128, NO, VK * D], fp32r)
        table_lo = sb("table_lo", [128, NO, VK * D], fp32r)
        vocab_sb = sb("vocab_sb", [128, VK])
        ident = sb("ident", [128, 128])
        XT = sb("XT", [128, J, S, FW])
        bottom_T = sb("bottom_T", [128, BLOCK])
        gram = sb("gram", [128, J, GW])
        pairs = sb("pairs", [J, S, ZW])
        pairs_T = sb("pairs_T", [128, ZC, BLOCK])
        h1 = sb("h1", [128, N1 // 128, BLOCK])
        h2 = sb("h2", [128, N2 // 128, BLOCK])
        y = sb("y", [1, BATCH])
        w1_sb = sb("w1_sb", [128, N1 // 128, N1])
        w2_sb = sb("w2_sb", [128, N1 // 128, N2])
        w3_sb = sb("w3_sb", [128, N2 // 128])
        b1_sb = sb("b1_sb", [128, N1 // 128])
        b2_sb = sb("b2_sb", [128, N2 // 128])

        psA = [pb(f"psA{i}", [128, 512]) for i in range(2)]
        psG = [pb(f"psG{i}", [128, 2, 512]) for i in range(2)]
        psC = [pb(f"psC{i}", [128, 512]) for i in range(2)]

        idx_ready = [sem(f"idx_ready{i}") for i in range(2)]
        rows_ready = [sem(f"rows_ready{p}") for p in range(NR)]
        bottom_ready = sem("bottom_ready")
        onehot_used = sem("onehot_used")
        ids_ready = [sem(f"ids_ready{i}") for i in range(NO)]
        onehot_made = sem("onehot_made")
        table_ready = [sem(f"table_ready{i}") for i in range(2)]
        hi_made = sem("hi_made")
        table_split = sem("table_split")
        consts_ready = sem("consts_ready")
        vocab_ready = sem("vocab_ready")
        weights_ready = sem("weights_ready")
        pads_set = sem("pads_set")
        a_full = [sem(f"a_full{i}") for i in range(2)]
        a_done = [sem(f"a_done{i}") for i in range(2)]
        g_full = sem("g_full")
        g_done = [sem(f"g_done{e}") for e in ("vector", "scalar")]
        c_full = [sem(f"c_full{i}") for i in range(2)]
        c_done = [sem(f"c_done{i}") for i in range(2)]
        out_done = sem("out_done")

        XT_by_feature = XT[:, :, :, :].rearrange("p j s f -> p f s j")

        def xt_views(kind, n):
            if kind == "bottom":
                return XT_by_feature[:, 0:1, :, :], psA[0][:, 0:BLOCK].rearrange("p (f s j) -> p f s j", s=S, j=J)
            a, b = ROWS[n] if kind == "rows" else ONEHOT[2 * n:2 * n + 2]
            src = psA[kind == "rows"][:, 0:2 * BLOCK].rearrange("p (f s j) -> p f s j", s=S, j=J)
            return XT_by_feature[:, a + 1:b + 2:b - a, :, :], src

        def a_count(bank, unit, m):
            return m * NA[bank] + (A_UNITS[bank].index(unit) + 1)

        def as_register(engine, count):
            return count if isinstance(count, int) else engine.to_reg(count)

        block = ctx.enter_context(nc.Block())

        @block.sync
        def _(sp):
            def load_idx(m, at, parity):
                sp.dma_start(idx[parity][:, :, :], ids[bass.ds(at, BLOCK), :].rearrange(
                    "(h p) f -> p h f", p=128)).then_inc(idx_ready[parity], 16)

            def load_bottom(at):
                sp.dma_start(bottom_rows[:, :, :], bottom[bass.ds(at, BLOCK), :].rearrange(
                    "(h p) d -> p h d", p=128)).then_inc(bottom_ready, 16)

            def load_ids(i, at):
                sp.dma_start(ids_bc[:, i, :], ids_by_table[ONEHOT[i]:ONEHOT[i] + 1, bass.ds(at, BLOCK)]
                             .partition_broadcast(128)).then_inc(ids_ready[i], 16)

            for m in range(2):
                load_idx(m, m * BLOCK, m)
            sp.dma_start(vocab_sb[0:VP, :], vocab).then_inc(vocab_ready, 16)
            for i in range(NO):
                load_ids(i, 0)
            sp.dma_start(ident[:, :], identity).then_inc(consts_ready, 16)
            load_bottom(0)
            for n, t in enumerate(ONEHOT):
                src = tables[t].rearrange("(p k) d -> p (k d)", k=VK)
                if n >= 2:
                    sp.wait_ge(table_split, n - 1)
                sp.dma_start(table_raw[0:112, n % 2, :], src[0:112, :]).then_inc(table_ready[n % 2], 16)
                sp.dma_start(table_raw[112:VP, n % 2, :], src[112:VP, :]).then_inc(table_ready[n % 2], 16)
            sp.dma_start(w1_sb[:, :, :], w1.rearrange("(t p) n -> p t n", p=128)).then_inc(weights_ready, 16)
            sp.dma_start(w2_sb[:, :, :], w2.rearrange("(t p) n -> p t n", p=128)).then_inc(weights_ready, 16)
            sp.dma_start(w3_sb[:, :], w3).then_inc(weights_ready, 16)
            sp.dma_start(b1_sb[:, :], b1).then_inc(weights_ready, 16)
            sp.dma_start(b2_sb[:, :], b2).then_inc(weights_ready, 16)
            for i in range(NOT_MADE_AHEAD):
                sp.wait_ge(onehot_made, i + 1)
                load_ids(i, BLOCK)

            def refill(m, parity, more=2):
                sp.wait_ge(a_full[0], a_count(0, ("bottom", 0), m))
                load_bottom((m + 1) * BLOCK)
                for i in range(NOT_MADE_AHEAD, NO):
                    sp.wait_ge(onehot_made, m * NO + i + 1)
                    load_ids(i, (m + 1) * BLOCK)
                if more >= 2:
                    for i in range(NOT_MADE_AHEAD):
                        sp.wait_ge(onehot_made, (m + 1) * NO + i + 1)
                        load_ids(i, (m + 2) * BLOCK)
                    sp.wait_ge(rows_ready[NR - 1], (m + 1) * 64)
                    load_idx(m + 2, (m + 2) * BLOCK, parity)

            with sp.Fori(0, BLOCKS // 2 - 1) as i:
                refill(i * 2, 0)
                refill(i * 2 + 1, 1)
            refill(BLOCKS - 2, 0, 1)
            sp.wait_ge(c_done[1], BLOCKS * NC)
            sp.dma_start(out.rearrange("b o -> o b"), y[0:1, :]).then_inc(out_done, 16)
            sp.wait_ge(out_done, 16)

        @block.gpsimd
        def _(pool):
            def gather_block(m, parity, visit, reuse=True):
                pool.wait_ge(idx_ready[parity], (visit + 1) * 16)
                for p, pair in enumerate(ROWS):
                    if reuse:
                        count = as_register(pool, a_count(1, ("rows", p), m - 1))
                        pool.wait_ge(idx_ready[parity], 16)
                        pool.wait_ge(a_full[1], count)
                    for n, t in enumerate(pair):
                        for h in range(HALVES):
                            nc.gpsimd.indirect_dma_start(
                                rows[:, p, n, h, :], None, tables[t],
                                bass.IndirectOffsetOnAxis(ap=idx[parity][:, h, t:t + 1], axis=0),
                            ).then_inc(rows_ready[p], 16)

            gather_block(0, 0, 0, reuse=False)
            gather_block(1, 1, 0)
            with pool.Fori(1, BLOCKS // 2) as i:
                gather_block(i * 2, 0, i)
                gather_block(i * 2 + 1, 1, i)

        @block.tensor
        def _(pe):
            def onehot_table(t, m, first):
                if t % 2 == 0 and not (first and t == 0):
                    pe.wait_ge(a_done[0], a_count(0, ("onehot", t // 2), m) - 1)
                if first:
                    pe.wait_ge(table_split, t + 1)
                pe.wait_ge(onehot_made, m * NO + t + 1)
                parts = [(part, k) for k in range(VK) for part in (table_hi, table_lo)]
                for q, (part, k) in enumerate(parts):
                    last = nc.tensor.matmul(psA[0][:, t % 2 * BLOCK:(t % 2 + 1) * BLOCK],
                                            part[0:VP, t, k * D:(k + 1) * D], onehot[0:VP, t % RING, k, :],
                                            start=(q == 0), stop=(q == len(parts) - 1))
                if t % 2 == 1:
                    last.then_inc(a_full[0], 1)
                else:
                    last.then_inc(onehot_used, 1)

            def bottom_output(m, first):
                pe.wait_ge(a_done[0], a_count(0, ("bottom", 0), m) - 1)
                if first:
                    pe.wait_ge(consts_ready, 16)
                pe.wait_ge(bottom_ready, (m + 1) * 16)
                for h in range(HALVES):
                    last = nc.tensor.transpose(psA[0][:, h * 128:(h + 1) * 128], bottom_rows[:, h, :], ident[:, :])
                last.then_inc(a_full[0], 1)

            def gathered_rows(p, m, first):
                if not (first and p == 0):
                    pe.wait_ge(a_done[1], a_count(1, ("rows", p), m) - 1)
                if first:
                    pe.wait_ge(consts_ready, 16)
                pe.wait_ge(rows_ready[p], (m + 1) * 64)
                for i in range(2):
                    for h in range(HALVES):
                        last = nc.tensor.transpose(psA[1][:, (i * HALVES + h) * 128:(i * HALVES + h + 1) * 128],
                                                   rows[:, p, i, h, :], ident[:, :])
                last.then_inc(a_full[1], 1)

            def phase_b(k, m, first):
                if k == 0:
                    for i in range(2):
                        pe.wait_ge(a_done[i], (m + 1) * NA[i])
                    if first:
                        pe.wait_ge(pads_set, 1)
                if not first or k >= 2:
                    for e in range(2):
                        pe.wait_ge(g_done[e], m * GSETS + k - 1)
                for i in range(8):
                    last = nc.tensor.matmul(psG[k % 2][:, i // 4, (i % 4) * S * GW:(i % 4 + 1) * S * GW],
                                            XT[:, 8 * k + i, :, :].rearrange("p s f -> p (s f)"), XT[:, 8 * k + i, :, 1:F],
                                            start=True, stop=True)
                last.then_inc(g_full, 1)

            def phase_c(u, m, first):
                kind, n = C_UNITS[u]
                bank = psC[u % 2]
                bank_free = as_register(pe, m * NC + u // 2)
                if kind == "columns":
                    grams_there = as_register(pe, (m + 1) * GSETS)
                    pe.wait_ge(consts_ready, 16)
                    if n == 0:
                        for i in range(2):
                            pe.wait_ge(g_done[i], grams_there)
                elif kind == "chunk":
                    columns_there = [as_register(pe, m * NC + 5 - i) for i in range(2)]
                    pe.wait_ge(pads_set, 1)
                    if n == 0:
                        for i in range(2):
                            pe.wait_ge(c_done[i], columns_there[i])
                if not first or u >= 2:
                    pe.wait_ge(c_done[u % 2], bank_free)
                if kind == "columns":
                    g0, count = GROUPS[n]
                    for i in range(count):
                        last = nc.tensor.transpose(bank[0:J, i * 128:(i + 1) * 128], gram[:, :, g0 - 1 + i], ident[:, :])
                elif kind == "chunk":
                    for s in range(S):
                        last = nc.tensor.transpose(bank[:, s * J:(s + 1) * J], pairs[:, s, n * 128:(n + 1) * 128],
                                                   ident[0:J, 0:J])
                elif kind == "layer1":
                    if n == 0:
                        if first:
                            pe.wait_ge(weights_ready, 5 * 16)
                        pe.wait_ge(c_done[0], m * NC + 6)
                        pe.wait_ge(c_done[1], m * NC + 6)
                    for i in range(2):
                        for t in range(ZC + 1):
                            last = nc.tensor.matmul(bank[:, i * BLOCK:(i + 1) * BLOCK],
                                                    w1_sb[:, t, (2 * n + i) * 128:(2 * n + i + 1) * 128],
                                                    pairs_T[:, t, :] if t < ZC else bottom_T[:, :],
                                                    start=(t == 0), stop=(t == ZC))
                elif kind == "layer2":
                    pe.wait_ge(c_done[0], m * NC + 7)
                    pe.wait_ge(c_done[1], m * NC + 7)
                    for i in range(2):
                        for t in range(N1 // 128):
                            last = nc.tensor.matmul(bank[:, i * BLOCK:(i + 1) * BLOCK],
                                                    w2_sb[:, t, i * 128:(i + 1) * 128], h1[:, t, :],
                                                    start=(t == 0), stop=(t == N1 // 128 - 1))
                else:
                    pe.wait_ge(c_done[0], m * NC + 8)
                    for t in range(N2 // 128):
                        last = nc.tensor.matmul(bank[0:1, 0:BLOCK], w3_sb[:, t:t + 1], h2[:, t, :],
                                                start=(t == 0), stop=(t == N2 // 128 - 1))
                last.then_inc(c_full[u % 2], 1)

            def block_steps(m, first=False, second=False):
                for step, n in STEPS:
                    if step == "onehot":
                        onehot_table(n, m, first)
                    elif step == "rows":
                        gathered_rows(n, m, first)
                    elif step == "bottom":
                        bottom_output(m, first)
                    elif step == "B":
                        phase_b(n, m, first)
                    elif not first:
                        phase_c(n, m - 1, second)

            block_steps(0, first=True)
            block_steps(1, second=True)
            with pe.Fori(2, BLOCKS) as m:
                block_steps(m)
            for u in range(len(C_UNITS)):
                phase_c(u, BLOCKS - 1, False)

        def gram_views(k, s):
            lanes = slice(FW * s, FW * (s + 1))
            src = psG[k % 2][lanes, :, 0:4 * S * GW].rearrange("p b (j s g) -> p b j s g", s=S, g=GW)[:, :, :, s, :]
            dst = gram[lanes, 8 * k:8 * k + 8, :].rearrange("p (b j) g -> p b j g", b=2)
            return dst, src

        def pair_views(n):
            g0, count = GROUPS[n]
            width = g0 + count - 1
            src = psC[n % 2][0:J, 0:count * 128].rearrange("p (g s f) -> p g s f", s=S, f=FW)[:, :, :, 0:width]
            dst = pairs[:, :, GROUP_AT[n]:GROUP_AT[n] + count * width].rearrange("p s (g f) -> p g s f", g=count)
            return dst, src

        @block.vector
        def _(dve):
            nc.vector.memset(XT[:, :, :, F:], 0.0)
            nc.vector.memset(pairs[:, :, ZUSED:], 0.0).then_inc(pads_set, 1)

            def make_onehot(t, m, first=False):
                dve.wait_ge(ids_ready[t], (m + 1) * 16)
                if not (first and t < RING):
                    before, block_of = (t - RING, m) if t >= RING else (t - RING + NO, m - 1)
                    if before % 2 == 1:
                        dve.wait_ge(a_full[0], a_count(0, ("onehot", before // 2), block_of))
                    else:
                        dve.wait_ge(onehot_used, block_of * (NO // 2) + before // 2 + 1)
                for k in range(VK):
                    last = nc.vector.tensor_scalar(onehot[0:VP, t % RING, k, :], ids_bc[0:VP, t, :],
                                                   vocab_sb[0:VP, k:k + 1], None, ALU.is_equal)
                last.then_inc(onehot_made, 1)

            def split_table(n):
                dve.wait_ge(hi_made, n + 1)
                nc.vector.tensor_tensor(table_lo[0:VP, n, :], table_raw[0:VP, n % 2, :],
                                        table_hi[0:VP, n, :].bitcast(fp32), ALU.subtract).then_inc(table_split, 1)

            dve.wait_ge(vocab_ready, 16)
            for n in range(NOT_MADE_AHEAD):
                make_onehot(n, 0, first=True)
                split_table(n)
            for n in range(NOT_MADE_AHEAD, NO):
                split_table(n)

            def phase_a(kind, n, m):
                dve.wait_ge(a_full[0], a_count(0, (kind, n), m))
                if kind == "bottom":
                    nc.vector.tensor_copy(bottom_T[:, :], psA[0][:, 0:BLOCK])
                dst, src = xt_views(kind, n)
                nc.vector.tensor_copy(dst, src).then_inc(a_done[0], 1)

            def phase_b(k, m):
                dve.wait_ge(g_full, m * GSETS + k + 1)
                for s in (0, 1):
                    dst, src = gram_views(k, s)
                    last = nc.vector.tensor_copy(dst, src)
                last.then_inc(g_done[0], 1)

            def phase_c(u, m):
                kind, n = C_UNITS[u]
                dve.wait_ge(c_full[0], m * NC + u // 2 + 1)
                if kind == "columns":
                    dst, src = pair_views(n)
                    last = nc.vector.tensor_copy(dst, src)
                elif kind == "chunk":
                    last = nc.vector.tensor_copy(pairs_T[:, n, :], psC[0][:, 0:BLOCK])
                else:
                    h, bias = (h1, b1_sb) if kind == "layer1" else (h2, b2_sb)
                    for i in range(2):
                        last = nc.vector.tensor_scalar(h[:, 2 * n + i, :], psC[0][:, i * BLOCK:(i + 1) * BLOCK],
                                                       bias[:, 2 * n + i:2 * n + i + 1], 0.0, ALU.add, ALU.max)
                last.then_inc(c_done[0], 1)

            def block_steps(m, first=False, second=False, final=False):
                if second:
                    dve.wait_ge(weights_ready, 5 * 16)
                for step, n in STEPS:
                    for t, ahead in MAKE.get((step, n), []):
                        if not (final and ahead):
                            make_onehot(t, m + ahead, first)
                    if step == "onehot" and n % 2 == 1:
                        phase_a("onehot", n // 2, m)
                    elif step == "bottom":
                        phase_a("bottom", 0, m)
                    elif step == "B":
                        phase_b(n, m)
                    elif step == "C" and not first and n % 2 == 0:
                        phase_c(n, m - 1)

            block_steps(0, first=True)
            block_steps(1, second=True)
            with dve.Fori(2, BLOCKS - 1) as m:
                block_steps(m)
            block_steps(BLOCKS - 1, final=True)
            for u in range(0, len(C_UNITS), 2):
                phase_c(u, BLOCKS - 1)

        @block.scalar
        def _(act):
            for n in range(NO):
                act.wait_ge(table_ready[n % 2], (n // 2 + 1) * 32)
                nc.scalar.copy(table_hi[0:VP, n, :], table_raw[0:VP, n % 2, :]).then_inc(hi_made, 1)

            def phase_a(p, m):
                act.wait_ge(a_full[1], a_count(1, ("rows", p), m))
                dst, src = xt_views("rows", p)
                nc.scalar.copy(dst, src).then_inc(a_done[1], 1)

            def phase_b(k, m):
                act.wait_ge(g_full, m * GSETS + k + 1)
                for s in (2, 3):
                    dst, src = gram_views(k, s)
                    last = nc.scalar.copy(dst, src)
                last.then_inc(g_done[1], 1)

            def phase_c(u, m):
                kind, n = C_UNITS[u]
                act.wait_ge(c_full[1], m * NC + u // 2 + 1)
                if kind == "columns":
                    dst, src = pair_views(n)
                    last = nc.scalar.copy(dst, src)
                elif kind == "chunk":
                    last = nc.scalar.copy(pairs_T[:, n, :], psC[1][:, 0:BLOCK])
                elif kind == "layer1":
                    for i in range(2):
                        last = nc.scalar.activation(h1[:, 2 * n + i, :], psC[1][:, i * BLOCK:(i + 1) * BLOCK],
                                                    ACT.Relu, bias=b1_sb[:, 2 * n + i:2 * n + i + 1])
                else:
                    last = nc.scalar.copy(y[0:1, bass.ds(m * BLOCK, BLOCK)], psC[1][0:1, 0:BLOCK])
                last.then_inc(c_done[1], 1)

            def block_steps(m, first=False, second=False):
                if second:
                    act.wait_ge(weights_ready, 5 * 16)
                for step, n in STEPS:
                    if step == "rows":
                        phase_a(n, m)
                    elif step == "B":
                        phase_b(n, m)
                    elif step == "C" and not first and n % 2 == 1:
                        phase_c(n, m - 1)

            block_steps(0, first=True)
            block_steps(1, second=True)
            with act.Fori(2, BLOCKS) as m:
                block_steps(m)
            for u in range(1, len(C_UNITS), 2):
                phase_c(u, BLOCKS - 1)


def w1_rows():
    rows = [-1] * ZW
    for (g0, count), at in zip(GROUPS, GROUP_AT):
        width = g0 + count - 1
        for i in range(count):
            for f in range(g0 + i):
                rows[at + i * width + f] = f * F - f * (f + 1) // 2 + (g0 + i - f - 1)
    pairs = F * (F - 1) // 2
    return rows + list(range(pairs, pairs + D))


def kernel(**inputs):
    import numpy as np
    import concourse.bacc as bacc
    from concourse.bass_utils import run_bass_kernel_spmd as run

    nc = bacc.Bacc("TRN2", target_bir_lowering=False, num_devices=1)
    src = np.array(w1_rows())
    w1 = np.zeros((ZW + D, N1), inputs["W_top1"].dtype)
    w1[src >= 0] = np.asarray(inputs["W_top1"])[src[src >= 0]]
    arrays = {
        "bottom": inputs["r_bottom_output"],
        "ids": inputs["ids"],
        "ids_by_table": np.asarray(inputs["ids"]).T,
        **{f"tbl_{t}": inputs[f"tbl_{t}"] for t in range(TABLES)},
        "w1": w1,
        "b1": np.asarray(inputs["b_top1"]).reshape(N1 // 128, 128).T,
        "w2": inputs["W_top2"],
        "b2": np.asarray(inputs["b_top2"]).reshape(N2 // 128, 128).T,
        "w3": np.asarray(inputs["W_top3"]).reshape(N2 // 128, 128).T,
        "identity": np.eye(128, dtype=np.float32),
        "vocab": np.arange(VP * VK, dtype=np.float32).reshape(VP, VK),
    }
    arrays = {f"in_{k}": np.ascontiguousarray(a) for k, a in arrays.items()}
    aps = {k[3:]: nc.dram_tensor(k, a.shape, mybir.dt.from_np(a.dtype), kind="ExternalInput").ap()
           for k, a in arrays.items()}
    out = nc.dram_tensor("out_y", (BATCH, 1), mybir.dt.float32, kind="ExternalOutput").ap()
    dlrm_tower(nc, aps["bottom"], aps["ids"], aps["ids_by_table"], [aps[f"tbl_{t}"] for t in range(TABLES)],
               aps["w1"], aps["b1"], aps["w2"], aps["b2"], aps["w3"], aps["identity"], aps["vocab"], out)
    return run(nc, [arrays], core_ids=[0]).results[0]["out_y"]
```

```python
import concourse.bass as bass
from concourse import mybir
from contextlib import ExitStack

TABLES = 26
F = TABLES + 1
D = 128
BATCH = 2048
N1, N2 = 512, 256

S, J = 4, 64
BLOCK = S * J
BLOCKS = BATCH // BLOCK
HALVES = BLOCK // 128
GM = S * F
GW = F - 1

ONEHOT = [6, 7, 8, 9, 10, 12]
RAW = 3
VP, VK = 125, 8
BUFFER = [0, 1, 2, 3, 0, 1, 2, 3, 2]
ROWS = [(0, 1), (2, 3), (4, 5), (11, 13), (14, 15), (17, 18), (16, 21), (19, 20), (22, 23), (24, 25)]
NO, NR = len(ONEHOT), len(ROWS)
EXTRA = 6
SHARED = 8
SHARED_TABLE = NO + 2
BY_ONEHOT = ONEHOT + list(ROWS[EXTRA]) + [ROWS[SHARED][0]]

GROUPS = [(g, 3) for g in range(1, 25, 3)] + [(25, 2)]


def group_columns():
    at, out = 0, []
    for g, n in GROUPS:
        out.append(at)
        at += n * (g + n - 1)
    return out, at


GROUP_AT, ZUSED = group_columns()
ZC = 3
ZW = ZC * 128

BOTTOM_AT = 7
A_UNITS = [[("onehot", n) for n in range(NO // 2)],
           [("rows", p) for p in range(BOTTOM_AT)] + [("bottom", 0)] + [("rows", p) for p in range(BOTTOM_AT, NR)]]
NA = [len(units) for units in A_UNITS]
C_UNITS = [("columns", q) for q in range(9)] + [("chunk", c) for c in range(ZC)] + \
          [("layer1", 0), ("layer1", 1), ("layer2", 0), ("layer3", 0)]
NC = len(C_UNITS) // 2
NHI = ZC + 4
GSETS = 8

STEPS = [("rows", 0), ("onehot", 0), ("C", 0), ("C", 1), ("rows", 1), ("C", 2), ("C", 3), ("onehot", (1, 0, 4)),
         ("C", 4), ("C", 5), ("onehot", (1, 4, 8)), ("C", 6), ("C", 7), ("rows", 2), ("onehot", (2, 0, 4)), ("C", 8),
         ("rows", 3), ("onehot", (2, 4, 8)), ("C", 9), ("rows", 4), ("C", 10), ("onehot", 3), ("C", 11), ("rows", 5),
         ("C", 12), ("rows", 6), ("C", 13), ("bottom", 0), ("onehot", 4), ("C", 14), ("rows", 7), ("onehot", (5, 0, 4)),
         ("rows", 8), ("onehot", (5, 4, 8)), ("rows", 9), ("C", 15)] + [("B", k) for k in range(GSETS)]
FIRST_STEPS = [("onehot", 0), ("rows", 0), ("onehot", 1), ("rows", 1), ("onehot", 2), ("rows", 2), ("onehot", 3),
               ("rows", 3), ("onehot", 4), ("rows", 4), ("onehot", 5), ("rows", 5), ("rows", EXTRA), ("bottom", 0)] + \
              [("rows", p) for p in range(EXTRA + 1, NR)] + [("B", k) for k in range(GSETS)]
LAST_OF_UNIT = [(1, 4, 8), 3, (5, 4, 8)]
ALL = range(VK)
MAKE = {("C", 0): [(2, 0, range(0, 4))], ("C", 1): [(2, 0, [4, 5])], ("C", 3): [(2, 0, [6, 7])],
        ("C", 12): [(4, 0, ALL)], ("C", 13): [(5, 0, ALL)], ("bottom", 0): [(SHARED_TABLE, 0, ALL)],
        ("rows", 7): [(3, 1, ALL)], ("C", 15): [(0, 1, ALL)],
        **{("B", k): [(1, 1, [k])] for k in range(GSETS)}}
MADE_AHEAD = (3, 0, 1)


def dlrm_tower(nc, bottom, ids, ids_by_table, tables, w1, b1, w2, b2, w3, identity, vocab, out):
    fp32, fp32r, i32 = mybir.dt.float32, mybir.dt.float32r, mybir.dt.int32
    ALU = mybir.AluOpType
    ACT = mybir.ActivationFunctionType

    ctx = ExitStack()
    with ctx:
        def sb(name, shape, dt=fp32):
            return ctx.enter_context(nc.sbuf_tensor(name, shape, dt))

        def pb(name, shape):
            return ctx.enter_context(nc.psum_tensor(name, shape, fp32))

        def sem(name):
            return ctx.enter_context(nc.semaphore(name))

        idx = [sb(f"idx{i}", [128, HALVES, TABLES], i32) for i in range(2)]
        rows = sb("rows", [128, NR, 2, HALVES, D])
        bottom_rows = sb("bottom_rows", [128, HALVES, D])
        ids_bc = sb("ids_bc", [128, len(BY_ONEHOT), BLOCK], i32)
        onehot = sb("onehot", [128, max(BUFFER) + 1, VK, BLOCK], fp32r)
        table_hi = sb("table_hi", [128, NO, VK * D], fp32r)
        table_lo = sb("table_lo", [128, NO, VK * D], fp32r)
        vocab_sb = sb("vocab_sb", [128, VK])
        ident = sb("ident", [128, 128])
        XT = sb("XT", [128, J, S, F])
        bottom_hi = sb("bottom_hi", [128, BLOCK], fp32r)
        bottom_lo = sb("bottom_lo", [128, BLOCK], fp32r)
        gram = sb("gram", [GM, J, GW])
        pairs = sb("pairs", [J, S, ZW])
        pairs_hi = sb("pairs_hi", [128, ZC, BLOCK], fp32r)
        pairs_lo = sb("pairs_lo", [128, ZC, BLOCK], fp32r)
        h1_hi = sb("h1_hi", [128, N1 // 128, BLOCK], fp32r)
        h1_lo = sb("h1_lo", [128, N1 // 128, BLOCK], fp32r)
        h2 = sb("h2", [128, N2 // 128, BLOCK])
        h1 = h2
        y = sb("y", [1, 2, BLOCK])
        w1_hi = sb("w1_hi", [128, N1 // 128, N1], fp32r)
        w1_lo = sb("w1_lo", [128, N1 // 128, N1], fp32r)
        w2_hi = sb("w2_hi", [128, N1 // 128, N2], fp32r)
        w2_lo = sb("w2_lo", [128, N1 // 128, N2], fp32r)
        w3_sb = sb("w3_sb", [128, N2 // 128])
        b1_sb = sb("b1_sb", [128, N1 // 128])
        b2_sb = sb("b2_sb", [128, N2 // 128])

        with nc.sbuf_tensor("raw", [128, RAW, VK * D], fp32) as raw:
            pass
        shared = sb("shared", [128, 2, VK * D], fp32r)

        psA = [pb(f"psA{i}", [128, 512]) for i in range(2)]
        psG = [pb(f"psG{i}", [128, 2, 512]) for i in range(2)]
        psC = [pb(f"psC{i}", [128, 512]) for i in range(2)]

        idx_ready = [sem(f"idx_ready{i}") for i in range(2)]
        rows_ready = [sem(f"rows_ready{p}") for p in range(NR)]
        bottom_ready = sem("bottom_ready")
        bottom_split = sem("bottom_split")
        ids_ready = [sem(f"ids_ready{i}") for i in range(len(BY_ONEHOT))]
        onehot_made = [sem(f"onehot_made{t}") for t in range(len(BY_ONEHOT))]
        onehot_used = [sem(f"onehot_used{t}") for t in range(NO)]
        raw_ready = [sem(f"raw_ready{i}") for i in range(RAW)]
        hi_made = sem("hi_made")
        raw_split = sem("raw_split")
        consts_ready = sem("consts_ready")
        vocab_ready = sem("vocab_ready")
        weights_ready = sem("weights_ready")
        pads_set = sem("pads_set")
        a_full = [sem(f"a_full{i}") for i in range(2)]
        a_done = [sem(f"a_done{i}") for i in range(2)]
        g_full = sem("g_full")
        g_part = [sem(f"g_part_{e}") for e in ("vector", "scalar")]
        g_done = [sem(f"g_done{e}") for e in ("vector", "scalar")]
        c_full = [sem(f"c_full{i}") for i in range(2)]
        c_hi_made = sem("c_hi_made")
        h1_split = sem("h1_split")
        c_done = [sem(f"c_done{i}") for i in range(2)]
        out_done = [sem(f"out_done{i}") for i in range(2)]

        XT_by_feature = XT[:, :, :, :].rearrange("p j s f -> p f s j")

        def xt_views(kind, n):
            if kind == "bottom":
                return XT_by_feature[:, 0:1, :, :], psA[1][:, 0:BLOCK].rearrange("p (f s j) -> p f s j", s=S, j=J)
            a, b = ROWS[n] if kind == "rows" else ONEHOT[2 * n:2 * n + 2]
            src = psA[kind == "rows"][:, 0:2 * BLOCK].rearrange("p (f s j) -> p f s j", s=S, j=J)
            return XT_by_feature[:, a + 1:b + 2:b - a, :, :], src

        def a_count(bank, unit, m):
            return m * NA[bank] + (A_UNITS[bank].index(unit) + 1)

        def c_bank(u, m):
            if isinstance(m, int) and m == BLOCKS - 1 and u < C_UNITS.index(("layer1", 0)):
                return (psC + psA)[u % 4]
            return psC[u % 2]

        def as_register(engine, count):
            return count if isinstance(count, int) else engine.to_reg(count)

        def table_parts(t):
            if t < NO:
                return table_hi[0:VP, t, :], table_lo[0:VP, t, :]
            if t == SHARED_TABLE:
                return [shared[0:VP, i, :] for i in (0, 1)]
            at = 2 * (t - NO)
            return [w[0:VP, at:at + 2, :].rearrange("p t n -> p (t n)") for w in (w1_hi, w1_lo)]

        def two_d(w):
            return w.rearrange("p t n -> p (t n)")

        w1_pieces = w1.rearrange("(i t p) n -> i p t n", i=2, p=128)
        PIECES = [(*table_parts(t), VP) for t in range(NO + 2)] + [(two_d(w2_hi[:, :, :]), two_d(w2_lo[:, :, :]), 128)] + \
                 [(two_d(w1_hi[:, i:i + 2, :]), two_d(w1_lo[:, i:i + 2, :]), 128) for i in (0, 2)] + \
                 [(*table_parts(SHARED_TABLE), VP)]
        assert (len(PIECES) - 1) % RAW == RAW - 1

        block = ctx.enter_context(nc.Block())

        @block.sync
        def _(sp):
            def load_idx(m, at, parity):
                sp.dma_start(idx[parity][:, :, :], ids[bass.ds(at, BLOCK), :].rearrange(
                    "(h p) f -> p h f", p=128)).then_inc(idx_ready[parity], 16)

            def load_bottom(at):
                sp.dma_start(bottom_rows[:, :, :], bottom[bass.ds(at, BLOCK), :].rearrange(
                    "(h p) d -> p h d", p=128)).then_inc(bottom_ready, 16)

            def load_ids(i, at):
                sp.dma_start(ids_bc[:, i, :], ids_by_table[BY_ONEHOT[i]:BY_ONEHOT[i] + 1, bass.ds(at, BLOCK)]
                             .partition_broadcast(128)).then_inc(ids_ready[i], 16)

            def load_piece(n):
                if n >= RAW:
                    sp.wait_ge(raw_split, n - RAW + 1)
                if n < NO + 2 or n == len(PIECES) - 1:
                    src = tables[BY_ONEHOT[min(n, SHARED_TABLE)]].rearrange("(p k) d -> p (k d)", k=VK)
                    sp.dma_start(raw[0:112, n % RAW, :], src[0:112, :]).then_inc(raw_ready[n % RAW], 16)
                    sp.dma_start(raw[112:VP, n % RAW, :], src[112:VP, :]).then_inc(raw_ready[n % RAW], 16)
                else:
                    src = w1_pieces[n - NO - 3] if n > NO + 2 else w2.rearrange("(t p) n -> p t n", p=128)
                    sp.dma_start(raw[:, n % RAW, :].rearrange("p (t n) -> p t n", t=src.shape[1]),
                                 src).then_inc(raw_ready[n % RAW], 32)

            load_idx(0, 0, 0)
            load_piece(0)
            sp.dma_start(vocab_sb[0:VP, :], vocab).then_inc(vocab_ready, 16)
            load_ids(0, 0)
            load_ids(1, 0)
            load_piece(1)
            sp.dma_start(ident[:, :], identity).then_inc(consts_ready, 16)
            load_piece(2)
            for i in range(2, NO + 2):
                load_ids(i, 0)
            load_idx(1, BLOCK, 1)
            load_bottom(0)
            for n in range(RAW, NO + 2):
                load_piece(n)
            for i in (2,) + MADE_AHEAD:
                sp.wait_ge(onehot_made[i], 1)
                load_ids(i, BLOCK)
            load_ids(SHARED_TABLE, BLOCK)
            for n in range(NO + 2, len(PIECES)):
                load_piece(n)
            sp.dma_start(w3_sb[:, :], w3).then_inc(weights_ready, 16)
            sp.dma_start(b1_sb[:, :], b1).then_inc(weights_ready, 16)
            sp.dma_start(b2_sb[:, :], b2).then_inc(weights_ready, 16)

            def store_y(m, parity):
                sp.wait_ge(c_done[1], (m + 1) * NC)
                sp.dma_start(out[bass.ds(m * BLOCK, BLOCK), :].rearrange("b o -> o b"),
                             y[:, parity, :]).then_inc(out_done[parity], 16)

            def refill(m, i, odd, first=False, two_ahead=True):
                for t in (4, 5) if first else (2, 4, 5):
                    sp.wait_ge(onehot_made[t], m + 1)
                    load_ids(t, (m + 1) * BLOCK)
                sp.wait_ge(a_full[1], a_count(1, ("bottom", 0), m))
                load_bottom((m + 1) * BLOCK)
                if odd:
                    sp.wait_ge(onehot_made[SHARED_TABLE], i + 1)
                    load_ids(SHARED_TABLE, (m + 2) * BLOCK)
                if two_ahead:
                    for t in MADE_AHEAD:
                        sp.wait_ge(onehot_made[t], m + 2)
                        load_ids(t, (m + 2) * BLOCK)
                    sp.wait_ge(rows_ready[NR - 1], (m + 1) * 64)
                    load_idx(m + 2, (m + 2) * BLOCK, odd)
                if not first:
                    store_y(m - 1, 1 - odd)

            refill(0, 0, 0, first=True)
            refill(1, 0, 1)
            with sp.Fori(1, BLOCKS // 2 - 1) as i:
                refill(i * 2, i, 0)
                refill(i * 2 + 1, i, 1)
            refill(BLOCKS - 2, BLOCKS // 2 - 1, 0, two_ahead=False)
            store_y(BLOCKS - 2, 0)
            store_y(BLOCKS - 1, 1)
            for parity in range(2):
                sp.wait_ge(out_done[parity], BLOCKS // 2 * 16)

        @block.gpsimd
        def _(pool):
            def gather_block(m, parity, visit, reuse=True):
                pool.wait_ge(idx_ready[parity], (visit + 1) * 16)
                for p, pair in enumerate(ROWS):
                    if p == EXTRA and not reuse:
                        continue
                    if reuse:
                        count = as_register(pool, a_count(1, ("rows", p), m - 1))
                        pool.wait_ge(idx_ready[parity], 16)
                        pool.wait_ge(a_full[1], count)
                    for n, t in enumerate(pair):
                        if (p, n) == (SHARED, 0) and parity == 1:
                            continue
                        for h in range(HALVES):
                            nc.gpsimd.indirect_dma_start(
                                rows[:, p, n, h, :], None, tables[t],
                                bass.IndirectOffsetOnAxis(ap=idx[parity][:, h, t:t + 1], axis=0),
                            ).then_inc(rows_ready[p], 16)

            gather_block(0, 0, 0, reuse=False)
            gather_block(1, 1, 0)
            with pool.Fori(1, BLOCKS // 2) as i:
                gather_block(i * 2, 0, i)
                gather_block(i * 2 + 1, 1, i)

        @block.tensor
        def _(pe):
            def onehot_products(features, t, slices):
                for k in slices:
                    for q, part in enumerate(table_parts(t)):
                        last = nc.tensor.matmul(features, part[:, k * D:(k + 1) * D], onehot[0:VP, BUFFER[t], k, :],
                                                start=(k == 0 and q == 0), stop=(k == VK - 1 and q == 1))
                return last

            def onehot_table(t, m, first, slices=ALL):
                if 0 in slices:
                    if t % 2 == 0 and not (first and t == 0):
                        pe.wait_ge(a_done[0], a_count(0, ("onehot", t // 2), m) - 1)
                    if first:
                        pe.wait_ge(raw_split, t + 1)
                    pe.wait_ge(onehot_made[t], m + 1)
                last = onehot_products(psA[0][:, t % 2 * BLOCK:(t % 2 + 1) * BLOCK], t, slices)
                if VK - 1 in slices:
                    last.then_inc(a_full[0] if t % 2 == 1 else onehot_used[t], 1)

            def bottom_output(m, first):
                pe.wait_ge(a_done[1], a_count(1, ("bottom", 0), m) - 1)
                if first:
                    pe.wait_ge(consts_ready, 16)
                pe.wait_ge(bottom_ready, (m + 1) * 16)
                for h in range(HALVES):
                    last = nc.tensor.transpose(psA[1][:, h * 128:(h + 1) * 128], bottom_rows[:, h, :], ident[:, :])
                last.then_inc(a_full[1], 1)

            def extra_tables(m):
                pe.wait_ge(a_done[1], a_count(1, ("rows", EXTRA), m) - 1)
                for i, t in enumerate((NO, NO + 1)):
                    pe.wait_ge(raw_split, t + 1)
                    pe.wait_ge(onehot_made[t], 1)
                    last = onehot_products(psA[1][:, i * BLOCK:(i + 1) * BLOCK], t, ALL)
                last.then_inc(a_full[1], 1)

            def gathered_rows(p, m, i, odd, first):
                if not (first and p == 0):
                    pe.wait_ge(a_done[1], a_count(1, ("rows", p), m) - 1)
                if first:
                    pe.wait_ge(consts_ready, 16)
                if p == SHARED and odd:
                    pe.wait_ge(raw_split, len(PIECES))
                    pe.wait_ge(onehot_made[SHARED_TABLE], i + 1)
                    onehot_products(psA[1][:, 0:BLOCK], SHARED_TABLE, ALL)
                if p == EXTRA:
                    pe.wait_ge(rows_ready[p], m * 64)
                elif p == SHARED:
                    pe.wait_ge(rows_ready[p], i * 96 + (96 if odd else 64))
                else:
                    pe.wait_ge(rows_ready[p], (m + 1) * 64)
                for n in range(1 if p == SHARED and odd else 0, 2):
                    for h in range(HALVES):
                        last = nc.tensor.transpose(psA[1][:, (n * HALVES + h) * 128:(n * HALVES + h + 1) * 128],
                                                   rows[:, p, n, h, :], ident[:, :])
                last.then_inc(a_full[1], 1)

            def phase_b(k, m, first):
                if k == 0:
                    for i in range(2):
                        pe.wait_ge(a_done[i], (m + 1) * NA[i])
                if not first or k >= 2:
                    for e in range(2):
                        pe.wait_ge(g_done[e], m * GSETS + k - 1)
                for i in range(8):
                    last = nc.tensor.matmul(psG[k % 2][0:GM, i // 4, (i % 4) * S * GW:(i % 4 + 1) * S * GW],
                                            XT[:, 8 * k + i, :, :].rearrange("p s f -> p (s f)"), XT[:, 8 * k + i, :, 1:F],
                                            start=True, stop=True)
                last.then_inc(g_full, 1)

            def layer(out_rows, w_hi, w_lo, n, features, chunks, ends):
                columns = slice(n * 128, (n + 1) * 128)
                products = [p for t in chunks for hi, lo in [features[t]]
                            for p in ((w_hi[:, t, columns], hi), (w_hi[:, t, columns], lo), (w_lo[:, t, columns], hi))]
                for q, (w, x) in enumerate(products):
                    last = nc.tensor.matmul(out_rows, w, x, start=(ends[0] and q == 0),
                                            stop=(ends[1] and q == len(products) - 1))
                return last

            def phase_c(u, m, first):
                kind, n = C_UNITS[u]
                bank = c_bank(u, m)
                four_banks = c_bank(2, m) is not psC[0] and 2 <= u < C_UNITS.index(("layer2", 0))
                bank_free = as_register(pe, m * NC + u // 2)
                if kind == "columns":
                    grams_there = as_register(pe, (m + 1) * GSETS)
                    pe.wait_ge(consts_ready, 16)
                    if n == 0:
                        for i in range(2):
                            pe.wait_ge(g_done[i], grams_there)
                elif kind == "chunk":
                    columns_there = [as_register(pe, m * NC + 5 - i) for i in range(2)]
                    pe.wait_ge(pads_set, 1)
                    if n == 0:
                        for i in range(2):
                            pe.wait_ge(c_done[i], columns_there[i])
                if four_banks:
                    if 4 <= u < C_UNITS.index(("layer1", 0)):
                        pe.wait_ge(c_done[u % 2], m * NC + (u - 4) // 2 + 1)
                elif not first or u >= 2:
                    pe.wait_ge(c_done[u % 2], bank_free)
                if kind == "columns":
                    g0, count = GROUPS[n]
                    for i in range(count):
                        last = nc.tensor.transpose(bank[0:J, i * GM:(i + 1) * GM], gram[:, :, g0 - 1 + i],
                                                   ident[0:GM, 0:GM])
                elif kind == "chunk":
                    for s in range(S):
                        last = nc.tensor.transpose(bank[:, s * J:(s + 1) * J], pairs[:, s, n * 128:(n + 1) * 128],
                                                   ident[0:J, 0:J])
                elif kind == "layer1":
                    if n == 0:
                        pe.wait_ge(bottom_split, m + 1)
                        if first:
                            pe.wait_ge(raw_split, len(PIECES) - 1)
                            pe.wait_ge(weights_ready, 3 * 16)
                    features = [(pairs_hi[:, t, :], pairs_lo[:, t, :]) for t in range(ZC)] + \
                               [(bottom_hi[:, :], bottom_lo[:, :])]
                    chunk_order = (ZC, 0, 1, 2)
                    for i in range(2):
                        for t in chunk_order:
                            if n == 0 and i == 0 and t < ZC:
                                unit = C_UNITS.index(("chunk", t))
                                pe.wait_ge(c_done[unit % 2], m * NC + (unit // 2 + 1))
                            last = layer(bank[:, i * BLOCK:(i + 1) * BLOCK], w1_hi, w1_lo, 2 * n + i, features,
                                         [t], (t == chunk_order[0], t == chunk_order[-1]))
                elif kind == "layer2":
                    features = [(h1_hi[:, t, :], h1_lo[:, t, :]) for t in range(N1 // 128)]
                    for i in range(2):
                        for t in range(N1 // 128):
                            if i == 0 and t % 2 == 0:
                                pe.wait_ge(h1_split, m * 2 + (t // 2 + 1))
                            elif i == 0:
                                pe.wait_ge(c_done[t // 2], m * NC + 7)
                            last = layer(bank[:, i * BLOCK:(i + 1) * BLOCK], w2_hi, w2_lo, i, features,
                                         [t], (t == 0, t == N1 // 128 - 1))
                else:
                    pe.wait_ge(c_done[0], m * NC + 8)
                    for t in range(N2 // 128):
                        last = nc.tensor.matmul(bank[0:1, 0:BLOCK], w3_sb[:, t:t + 1], h2[:, t, :],
                                                start=(t == 0), stop=(t == N2 // 128 - 1))
                last.then_inc(c_full[u % 2], 1)

            def block_steps(m, i, odd, first=False, second=False):
                for step, n in FIRST_STEPS if first else STEPS:
                    if first and (step, n) == ("rows", EXTRA):
                        extra_tables(m)
                    elif step == "onehot":
                        if isinstance(n, tuple):
                            onehot_table(n[0], m, first, range(n[1], n[2]))
                        else:
                            onehot_table(n, m, first)
                    elif step == "rows":
                        gathered_rows(n, m, i, odd, first)
                    elif step == "bottom":
                        bottom_output(m, first)
                    elif step == "B":
                        phase_b(n, m, first)
                    elif not first:
                        phase_c(n, m - 1, second)

            block_steps(0, 0, 0, first=True)
            block_steps(1, 0, 1, second=True)
            with pe.Fori(1, BLOCKS // 2) as i:
                block_steps(i * 2, i, 0)
                block_steps(i * 2 + 1, i, 1)
            for u in range(len(C_UNITS)):
                phase_c(u, BLOCKS - 1, False)

        def gram_views(k, b, s):
            rows_to = F * (s + 1)
            src = psG[k % 2][0:rows_to, b, 0:4 * S * GW].rearrange("p (j s g) -> p j s g", s=S, g=GW)[:, :, s, :]
            return gram[0:rows_to, 8 * k + 4 * b:8 * k + 4 * b + 4, :], src

        def parts(k, s, m):
            return (m * GSETS + k) * (S - 1) + (S - s)

        def pair_views(n, m):
            g0, count = GROUPS[n]
            width = g0 + count - 1
            src = c_bank(n, m)[0:J, 0:count * GM].rearrange("p (g s f) -> p g s f", s=S, f=F)[:, :, :, 0:width]
            dst = pairs[:, :, GROUP_AT[n]:GROUP_AT[n] + count * width].rearrange("p s (g f) -> p g s f", g=count)
            return dst, src

        @block.vector
        def _(dve):
            nc.vector.memset(pairs[:, :, ZUSED:], 0.0).then_inc(pads_set, 1)

            def make_onehot(t, m, slices=ALL, first=False, visit=None):
                if 0 in slices:
                    dve.wait_ge(ids_ready[t], ((m if visit is None else visit) + 1) * 16)
                if 0 not in slices or (first and t < 4):
                    pass
                elif t == 0:
                    dve.wait_ge(onehot_used[4], m)
                elif t == 1:
                    dve.wait_ge(a_full[0], a_count(0, ("onehot", 2), m - 1))
                elif t == 2:
                    dve.wait_ge(a_full[1], a_count(1, ("rows", SHARED), m - 1))
                elif t == 3:
                    dve.wait_ge(a_full[0], a_count(0, ("onehot", 1), m - 1))
                elif t == SHARED_TABLE:
                    dve.wait_ge(onehot_used[2], m + 1)
                elif t % 2 == 1:
                    dve.wait_ge(a_full[0], a_count(0, ("onehot", (t - 4) // 2), m))
                else:
                    dve.wait_ge(onehot_used[t - 4], m + 1)
                for k in slices:
                    last = nc.vector.tensor_scalar(onehot[0:VP, BUFFER[t], k, :], ids_bc[0:VP, t, :],
                                                   vocab_sb[0:VP, k:k + 1], None, ALU.is_equal)
                if VK - 1 in slices:
                    last.then_inc(onehot_made[t], 1)

            def split_piece(n):
                hi, lo, lanes = PIECES[n]
                dve.wait_ge(hi_made, n + 1)
                nc.vector.tensor_tensor(lo, raw[0:lanes, n % RAW, :], hi.bitcast(fp32),
                                        ALU.subtract).then_inc(raw_split, 1)

            def phase_a(n, m):
                dve.wait_ge(a_full[0], a_count(0, ("onehot", n), m))
                dst, src = xt_views("onehot", n)
                nc.vector.tensor_copy(dst, src).then_inc(a_done[0], 1)

            def bottom_output(m):
                dve.wait_ge(a_done[1], a_count(1, ("bottom", 0), m))
                nc.vector.tensor_tensor(bottom_lo[:, :].rearrange("p (s j) -> p s j", s=S),
                                        XT[:, :, :, 0].rearrange("p j s -> p s j"),
                                        bottom_hi[:, :].bitcast(fp32).rearrange("p (s j) -> p s j", s=S),
                                        ALU.subtract).then_inc(bottom_split, 1)

            def phase_b(k, m):
                dve.wait_ge(g_full, m * GSETS + k + 1)
                for s in reversed(range(S)):
                    dst, src = gram_views(k, 0, s)
                    if s < S - 1:
                        dve.wait_ge(g_part[0], parts(k, s + 1, m))
                    nc.vector.tensor_copy(dst, src).then_inc(g_part[0] if s else g_done[0], 1)

            def phase_c(u, m):
                kind, n = C_UNITS[u]
                if kind == "chunk":
                    dve.wait_ge(c_hi_made, m * NHI + n + 1)
                    nc.vector.tensor_tensor(pairs_lo[:, n, :], c_bank(u, m)[:, 0:BLOCK],
                                            pairs_hi[:, n, :].bitcast(fp32), ALU.subtract).then_inc(c_done[u % 2], 1)
                elif kind == "layer1":
                    for i in range(2):
                        dve.wait_ge(c_hi_made, m * NHI + (ZC + 2 * n + i + 1))
                        nc.vector.tensor_tensor(h1_lo[:, 2 * n + i, :], h1[:, i, :], h1_hi[:, 2 * n + i, :].bitcast(fp32),
                                                ALU.subtract).then_inc(c_done[u % 2] if i else h1_split, 1)
                elif u % 2 == 0:
                    dve.wait_ge(c_full[0], m * NC + u // 2 + 1)
                    if kind == "columns":
                        dst, src = pair_views(n, m)
                        last = nc.vector.tensor_copy(dst, src)
                    else:
                        for i in range(2):
                            last = nc.vector.tensor_scalar(h2[:, i, :], psC[0][:, i * BLOCK:(i + 1) * BLOCK],
                                                           b2_sb[:, i:i + 1], 0.0, ALU.add, ALU.max)
                    last.then_inc(c_done[0], 1)

            def first_block():
                dve.wait_ge(vocab_ready, 16)
                for t in range(NO + 2):
                    split_piece(t)
                    make_onehot(t, 0, first=True)
                    if t in (2, 4):
                        phase_a((t - 2) // 2, 0)
                phase_a(2, 0)
                split_piece(NO + 2)
                dve.wait_ge(a_full[1], a_count(1, ("rows", EXTRA), 0))
                bottom_output(0)
                make_onehot(3, 1)
                split_piece(NO + 3)
                make_onehot(0, 1)
                split_piece(NO + 4)
                dve.wait_ge(raw_split, len(PIECES) - 1)
                split_piece(NO + 5)
                for k in range(GSETS):
                    make_onehot(1, 1, [k])
                    phase_b(k, 0)

            def block_steps(m, i, odd, second=False, final=False):
                if second:
                    dve.wait_ge(weights_ready, 3 * 16)
                for step, n in STEPS:
                    for t, ahead, slices in MAKE.get((step, n), []):
                        if t == SHARED_TABLE:
                            if odd:
                                make_onehot(t, m, visit=i)
                        elif not (final and ahead):
                            make_onehot(t, m + ahead, slices)
                    if step == "onehot" and n in LAST_OF_UNIT:
                        phase_a(LAST_OF_UNIT.index(n), m)
                    elif step == "bottom":
                        bottom_output(m)
                    elif step == "B":
                        phase_b(n, m)
                    elif step == "C":
                        phase_c(n, m - 1)

            first_block()
            block_steps(1, 0, 1, second=True)
            with dve.Fori(1, BLOCKS // 2 - 1) as i:
                block_steps(i * 2, i, 0)
                block_steps(i * 2 + 1, i, 1)
            block_steps(BLOCKS - 2, BLOCKS // 2 - 1, 0)
            block_steps(BLOCKS - 1, BLOCKS // 2 - 1, 1, final=True)
            for u in range(len(C_UNITS)):
                phase_c(u, BLOCKS - 1)

        @block.scalar
        def _(act):
            def split_piece(n):
                hi, lo, lanes = PIECES[n]
                act.wait_ge(raw_ready[n % RAW], (n // RAW + 1) * 32)
                nc.scalar.copy(hi, raw[0:lanes, n % RAW, :]).then_inc(hi_made, 1)

            def phase_a(kind, n, m):
                act.wait_ge(a_full[1], a_count(1, (kind, n), m))
                if kind == "bottom":
                    nc.scalar.copy(bottom_hi[:, :], psA[1][:, 0:BLOCK])
                dst, src = xt_views(kind, n)
                nc.scalar.copy(dst, src).then_inc(a_done[1], 1)

            def phase_b(k, m):
                act.wait_ge(g_full, m * GSETS + k + 1)
                for s in reversed(range(S)):
                    dst, src = gram_views(k, 1, s)
                    if s < S - 1:
                        act.wait_ge(g_part[1], parts(k, s + 1, m))
                    nc.scalar.copy(dst, src).then_inc(g_part[1] if s else g_done[1], 1)

            def phase_c(u, m, visit, parity):
                kind, n = C_UNITS[u]
                if kind == "chunk":
                    act.wait_ge(c_full[u % 2], m * NC + u // 2 + 1)
                    nc.scalar.copy(pairs_hi[:, n, :], c_bank(u, m)[:, 0:BLOCK]).then_inc(c_hi_made, 1)
                elif kind == "layer1":
                    act.wait_ge(c_full[u % 2], m * NC + u // 2 + 1)
                    if n == 1:
                        act.wait_ge(c_done[0], m * NC + 7)
                    for i in range(2):
                        for h in (h1[:, i, :], h1_hi[:, 2 * n + i, :]):
                            last = nc.scalar.activation(h, psC[u % 2][:, i * BLOCK:(i + 1) * BLOCK],
                                                        ACT.Relu, bias=b1_sb[:, 2 * n + i:2 * n + i + 1])
                        last.then_inc(c_hi_made, 1)
                elif u % 2 == 1:
                    act.wait_ge(c_full[1], m * NC + u // 2 + 1)
                    if kind == "columns":
                        dst, src = pair_views(n, m)
                        last = nc.scalar.copy(dst, src)
                    else:
                        if not (isinstance(visit, int) and visit == 0):
                            act.wait_ge(out_done[parity], visit * 16)
                        last = nc.scalar.copy(y[:, parity, :], psC[1][0:1, 0:BLOCK])
                    last.then_inc(c_done[1], 1)

            def block_steps(m, i, odd, first=False, second=False):
                if second:
                    act.wait_ge(weights_ready, 3 * 16)
                if first:
                    for n in range(4):
                        split_piece(n)
                SPLIT_HERE = [("rows", 1), ("rows", 2), ("rows", 3), ("rows", 4), ("rows", EXTRA),
                              ("rows", EXTRA + 2), ("rows", EXTRA + 3), ("B", 0)]
                for step, n in FIRST_STEPS if first else STEPS:
                    if first and (step, n) in SPLIT_HERE:
                        if step == "B":
                            act.wait_ge(raw_split, len(PIECES) - 2)
                        split_piece(4 + SPLIT_HERE.index((step, n)))
                    if step in ("rows", "bottom"):
                        phase_a(step, n, m)
                    elif step == "B":
                        phase_b(n, m)
                    elif step == "C" and not first:
                        phase_c(n, m - 1, i if odd else i - 1, 1 - odd)

            block_steps(0, 0, 0, first=True)
            block_steps(1, 0, 1, second=True)
            block_steps(2, 1, 0)
            block_steps(3, 1, 1)
            with act.Fori(2, BLOCKS // 2) as i:
                block_steps(i * 2, i, 0)
                block_steps(i * 2 + 1, i, 1)
            for u in range(len(C_UNITS)):
                phase_c(u, BLOCKS - 1, BLOCKS // 2 - 1, 1)


def w1_rows():
    rows = [-1] * ZW
    for (g0, count), at in zip(GROUPS, GROUP_AT):
        width = g0 + count - 1
        for i in range(count):
            for f in range(g0 + i):
                rows[at + i * width + f] = f * F - f * (f + 1) // 2 + (g0 + i - f - 1)
    pairs = F * (F - 1) // 2
    return rows + list(range(pairs, pairs + D))


def kernel(**inputs):
    import numpy as np
    import concourse.bacc as bacc
    from concourse.bass_utils import run_bass_kernel_spmd as run

    nc = bacc.Bacc("TRN2", target_bir_lowering=False, num_devices=1)
    src = np.array(w1_rows())
    w1 = np.zeros((ZW + D, N1), inputs["W_top1"].dtype)
    w1[src >= 0] = np.asarray(inputs["W_top1"])[src[src >= 0]]
    arrays = {
        "bottom": inputs["r_bottom_output"],
        "ids": inputs["ids"],
        "ids_by_table": np.asarray(inputs["ids"]).T,
        **{f"tbl_{t}": inputs[f"tbl_{t}"] for t in range(TABLES)},
        "w1": w1,
        "b1": np.asarray(inputs["b_top1"]).reshape(N1 // 128, 128).T,
        "w2": inputs["W_top2"],
        "b2": np.asarray(inputs["b_top2"]).reshape(N2 // 128, 128).T,
        "w3": np.asarray(inputs["W_top3"]).reshape(N2 // 128, 128).T,
        "identity": np.eye(128, dtype=np.float32),
        "vocab": np.arange(VP * VK, dtype=np.float32).reshape(VP, VK),
    }
    arrays = {f"in_{k}": np.ascontiguousarray(a) for k, a in arrays.items()}
    aps = {k[3:]: nc.dram_tensor(k, a.shape, mybir.dt.from_np(a.dtype), kind="ExternalInput").ap()
           for k, a in arrays.items()}
    out = nc.dram_tensor("out_y", (BATCH, 1), mybir.dt.float32, kind="ExternalOutput").ap()
    dlrm_tower(nc, aps["bottom"], aps["ids"], aps["ids_by_table"], [aps[f"tbl_{t}"] for t in range(TABLES)],
               aps["w1"], aps["b1"], aps["w2"], aps["b2"], aps["w3"], aps["identity"], aps["vocab"], out)
    return run(nc, [arrays], core_ids=[0]).results[0]["out_y"]
```
